# Optimizing a Trainium2 kernel written in Bass

```python
import numpy as np
import jax
import jax.numpy as jnp

def _softmax(x, axis=-1):
    return jax.nn.softmax(x, axis=axis)

def _gelu(x):
    return jax.nn.gelu(x, approximate=True)

def _silu(x):
    return jax.nn.silu(x)

def _sigmoid(x):
    return jax.nn.sigmoid(x)

def _layernorm(x, axis=-1, eps=1e-05):
    m = jnp.mean(x, axis=axis, keepdims=True)
    v = jnp.var(x, axis=axis, keepdims=True)
    return (x - m) / jnp.sqrt(v + eps)

def _scatter_add(tgt, idx, src, axis=0):
    return tgt.at[idx].add(src)

def _segment_sum(src, seg, n):
    return jax.ops.segment_sum(src, seg, n)
kernel_name = 'mk_dlrm_tower_d1_rec_r8_e0dba3'

def setup_inputs(seed: int=0):
    np.random.seed(seed)
    _w = jnp.asarray

    def _rec_inputs():
        import jax
        import jax.numpy as jnp
        _tk = jax.random.key(seed)
        ids = jnp.stack([jax.random.randint(jax.random.fold_in(_tk, 200 + f), (512,), 0, v, jnp.int32) for f, v in enumerate([125000, 1000, 1250, 1250, 12500, 1000, 1250, 12500, 1000, 12500, 1250, 12500, 12500, 12500, 12500, 12500, 12500, 1000, 1000, 1000, 1000, 1000, 1000, 1000, 1000, 1000])], axis=1)
        tbl_0 = 0.05 * jax.random.normal(jax.random.fold_in(_tk, 500 + 0), (125000, 128), jnp.float32)
        tbl_1 = 0.05 * jax.random.normal(jax.random.fold_in(_tk, 500 + 1), (1000, 128), jnp.float32)
        tbl_2 = 0.05 * jax.random.normal(jax.random.fold_in(_tk, 500 + 2), (1250, 128), jnp.float32)
        tbl_3 = 0.05 * jax.random.normal(jax.random.fold_in(_tk, 500 + 3), (1250, 128), jnp.float32)
        tbl_4 = 0.05 * jax.random.normal(jax.random.fold_in(_tk, 500 + 4), (12500, 128), jnp.float32)
        tbl_5 = 0.05 * jax.random.normal(jax.random.fold_in(_tk, 500 + 5), (1000, 128), jnp.float32)
        tbl_6 = 0.05 * jax.random.normal(jax.random.fold_in(_tk, 500 + 6), (1250, 128), jnp.float32)
        tbl_7 = 0.05 * jax.random.normal(jax.random.fold_in(_tk, 500 + 7), (12500, 128), jnp.float32)
        tbl_8 = 0.05 * jax.random.normal(jax.random.fold_in(_tk, 500 + 8), (1000, 128), jnp.float32)
        tbl_9 = 0.05 * jax.random.normal(jax.random.fold_in(_tk, 500 + 9), (12500, 128), jnp.float32)
        tbl_10 = 0.05 * jax.random.normal(jax.random.fold_in(_tk, 500 + 10), (1250, 128), jnp.float32)
        tbl_11 = 0.05 * jax.random.normal(jax.random.fold_in(_tk, 500 + 11), (12500, 128), jnp.float32)
        tbl_12 = 0.05 * jax.random.normal(jax.random.fold_in(_tk, 500 + 12), (12500, 128), jnp.float32)
        tbl_13 = 0.05 * jax.random.normal(jax.random.fold_in(_tk, 500 + 13), (12500, 128), jnp.float32)
        tbl_14 = 0.05 * jax.random.normal(jax.random.fold_in(_tk, 500 + 14), (12500, 128), jnp.float32)
        tbl_15 = 0.05 * jax.random.normal(jax.random.fold_in(_tk, 500 + 15), (12500, 128), jnp.float32)
        tbl_16 = 0.05 * jax.random.normal(jax.random.fold_in(_tk, 500 + 16), (12500, 128), jnp.float32)
        tbl_17 = 0.05 * jax.random.normal(jax.random.fold_in(_tk, 500 + 17), (1000, 128), jnp.float32)
        tbl_18 = 0.05 * jax.random.normal(jax.random.fold_in(_tk, 500 + 18), (1000, 128), jnp.float32)
        tbl_19 = 0.05 * jax.random.normal(jax.random.fold_in(_tk, 500 + 19), (1000, 128), jnp.float32)
        tbl_20 = 0.05 * jax.random.normal(jax.random.fold_in(_tk, 500 + 20), (1000, 128), jnp.float32)
        tbl_21 = 0.05 * jax.random.normal(jax.random.fold_in(_tk, 500 + 21), (1000, 128), jnp.float32)
        tbl_22 = 0.05 * jax.random.normal(jax.random.fold_in(_tk, 500 + 22), (1000, 128), jnp.float32)
        tbl_23 = 0.05 * jax.random.normal(jax.random.fold_in(_tk, 500 + 23), (1000, 128), jnp.float32)
        tbl_24 = 0.05 * jax.random.normal(jax.random.fold_in(_tk, 500 + 24), (1000, 128), jnp.float32)
        tbl_25 = 0.05 * jax.random.normal(jax.random.fold_in(_tk, 500 + 25), (1000, 128), jnp.float32)
        _rk = jax.random.fold_in(_tk, 7)
        r_dense_features = -0.000520686 + 1.00062 * jax.random.normal(jax.random.fold_in(_rk, 101), (512, 128), jnp.float32)
        W_top1 = 0.0405887 * jax.random.normal(jax.random.fold_in(_tk, 801), (607, 512), jnp.float32)
        W_top2 = 0.0441942 * jax.random.normal(jax.random.fold_in(_tk, 802), (512, 256), jnp.float32)
        W_top3 = 0.0625 * jax.random.normal(jax.random.fold_in(_tk, 803), (256, 1), jnp.float32)
        b_top1 = jnp.zeros((512,), jnp.float32)
        b_top2 = jnp.zeros((256,), jnp.float32)
        return (r_dense_features, ids, tbl_0, tbl_1, tbl_2, tbl_3, tbl_4, tbl_5, tbl_6, tbl_7, tbl_8, tbl_9, tbl_10, tbl_11, tbl_12, tbl_13, tbl_14, tbl_15, tbl_16, tbl_17, tbl_18, tbl_19, tbl_20, tbl_21, tbl_22, tbl_23, tbl_24, tbl_25, W_top1, b_top1, W_top2, b_top2, W_top3)
    r_dense_features, ids, tbl_0, tbl_1, tbl_2, tbl_3, tbl_4, tbl_5, tbl_6, tbl_7, tbl_8, tbl_9, tbl_10, tbl_11, tbl_12, tbl_13, tbl_14, tbl_15, tbl_16, tbl_17, tbl_18, tbl_19, tbl_20, tbl_21, tbl_22, tbl_23, tbl_24, tbl_25, W_top1, b_top1, W_top2, b_top2, W_top3 = _rec_inputs()

    def _L0_rec_setup():
        import jax, jax.numpy as jnp
        import numpy as np
        B, F, D = (2048, 26, 128)
        key = jax.random.key(seed)
        k1, k2 = jax.random.split(key)
        dense_features = jax.random.normal(k1, (B, D), dtype=jnp.float32)
        sparse_values = jax.random.normal(k2, (B, F, D), dtype=jnp.float32)
        return {'dense_features': dense_features, 'sparse_values': sparse_values}
    _L0_rec_all = _L0_rec_setup()
    _L0_rec_in = {k: v for k, v in _L0_rec_all.items() if k in ()}
    del _L0_rec_all
    return {'r_dense_features': r_dense_features, 'ids': ids, 'tbl_0': tbl_0, 'tbl_1': tbl_1, 'tbl_2': tbl_2, 'tbl_3': tbl_3, 'tbl_4': tbl_4, 'tbl_5': tbl_5, 'tbl_6': tbl_6, 'tbl_7': tbl_7, 'tbl_8': tbl_8, 'tbl_9': tbl_9, 'tbl_10': tbl_10, 'tbl_11': tbl_11, 'tbl_12': tbl_12, 'tbl_13': tbl_13, 'tbl_14': tbl_14, 'tbl_15': tbl_15, 'tbl_16': tbl_16, 'tbl_17': tbl_17, 'tbl_18': tbl_18, 'tbl_19': tbl_19, 'tbl_20': tbl_20, 'tbl_21': tbl_21, 'tbl_22': tbl_22, 'tbl_23': tbl_23, 'tbl_24': tbl_24, 'tbl_25': tbl_25, 'W_top1': W_top1, 'b_top1': b_top1, 'W_top2': W_top2, 'b_top2': b_top2, 'W_top3': W_top3}

def reference(r_dense_features, ids, tbl_0, tbl_1, tbl_2, tbl_3, tbl_4, tbl_5, tbl_6, tbl_7, tbl_8, tbl_9, tbl_10, tbl_11, tbl_12, tbl_13, tbl_14, tbl_15, tbl_16, tbl_17, tbl_18, tbl_19, tbl_20, tbl_21, tbl_22, tbl_23, tbl_24, tbl_25, W_top1, b_top1, W_top2, b_top2, W_top3):
    import jax
    import jax.numpy as jnp

    def _L0_rec_ref(dense_features, sparse_values):
        import jax, jax.numpy as jnp
        import numpy as np
        B, F, D = (2048, 26, 128)
        sd = jnp.einsum('bfd,bd->bf', sparse_values, dense_features)
        ss = jnp.einsum('bfd,bgd->bfg', sparse_values, sparse_values)
        iu, ju = jnp.triu_indices(F, k=1)
        pairs = ss[:, iu, ju]
        return jnp.concatenate([dense_features, sd, pairs], axis=1)
    e = jnp.stack([tbl_0[ids[:, 0]], tbl_1[ids[:, 1]], tbl_2[ids[:, 2]], tbl_3[ids[:, 3]], tbl_4[ids[:, 4]], tbl_5[ids[:, 5]], tbl_6[ids[:, 6]], tbl_7[ids[:, 7]], tbl_8[ids[:, 8]], tbl_9[ids[:, 9]], tbl_10[ids[:, 10]], tbl_11[ids[:, 11]], tbl_12[ids[:, 12]], tbl_13[ids[:, 13]], tbl_14[ids[:, 14]], tbl_15[ids[:, 15]], tbl_16[ids[:, 16]], tbl_17[ids[:, 17]], tbl_18[ids[:, 18]], tbl_19[ids[:, 19]], tbl_20[ids[:, 20]], tbl_21[ids[:, 21]], tbl_22[ids[:, 22]], tbl_23[ids[:, 23]], tbl_24[ids[:, 24]], tbl_25[ids[:, 25]]], axis=1)
    z = _L0_rec_ref(r_dense_features, e)
    z = z.reshape(z.shape[0], -1)
    h = jnp.concatenate([z, r_dense_features], axis=1)
    h = jnp.maximum(h @ W_top1 + b_top1, 0.0)
    h = jnp.maximum(h @ W_top2 + b_top2, 0.0)
    y = h @ W_top3
    return y

_drawn_inputs = setup_inputs


def setup_inputs(seed=0):
    import zlib

    import numpy as np

    out = dict(_drawn_inputs(seed))
    spreads = {'b_top1': (0.0, 0.1), 'b_top2': (0.0, 0.1)}
    factors = {}
    for name, (base, spread) in spreads.items():
        noise = np.random.default_rng([zlib.crc32(name.encode()), seed]).standard_normal(out[name].shape)
        drawn = base * np.exp(spread * noise) if base else spread * noise
        out[name] = jnp.asarray(drawn.astype(out[name].dtype))
    for name, factor in factors.items():
        out[name] = (out[name] * factor).astype(out[name].dtype)
    return out
```

```python
from contextlib import ExitStack

import numpy as np

import concourse.bass as bass
from concourse import mybir

F32 = mybir.dt.float32
I32 = mybir.dt.int32
U32 = mybir.dt.uint32
ALU = mybir.AluOpType
ACT = mybir.ActivationFunctionType

P = 128
PER_BANK = 4
QUADRANT = 32
GROUPS = P // QUADRANT


def column_groups(slots):
    out, place = [], 0
    for first, count in [(0, 2), (2, 2)] + [(c, 4) for c in range(4, slots - 3, 4)] + [(slots - 3, 2)]:
        rows = slots - 1 - first
        out.append((first, count, first + 1, rows, place))
        place += count * rows
    return out, place


def build_dlrm_tower(nc, dense, ids, tables, w_top1, b_top1, w_top2, b_top2, w_top3, out):
    B, D = dense.shape
    F = ids.shape[1]
    H1, H2 = w_top2.shape
    TILES = B // P
    HALVES = 2
    SLOTS = F + 1
    LOTS = -(-SLOTS // PER_BANK)
    QUADS = P // GROUPS
    PER_GRAM_BANK = QUADS // 2
    BLOCKS, PAIR_ROWS = column_groups(SLOTS)
    CHUNKS = PAIR_ROWS // P
    M1, M2 = H1 // P, H2 // P
    assert D == P and B % (P * HALVES) == 0 and PAIR_ROWS % P == 0 and H1 % P == 0 and H2 % P == 0
    assert PER_GRAM_BANK * QUADRANT == 512 and M1 * P == 512
    PAIRS0 = D
    DENSE1 = PAIRS0 + SLOTS * (SLOTS - 1) // 2
    assert w_top1.shape[0] == DENSE1 + D

    def lot(k):
        return range(PER_BANK * k, min(PER_BANK * (k + 1), SLOTS))

    weight_runs = []
    for first, count, _, rows, place in BLOCKS:
        for i in range(count):
            c = first + i
            src = PAIRS0 + sum(SLOTS - 1 - k for k in range(c))
            dst, n = place + i * rows + i, rows - i
            while n:
                m = min(n, P - dst % P)
                weight_runs.append((src, dst, m))
                src, dst, n = src + m, dst + m, n - m

    dense_v = dense.rearrange("(p t) d -> p t d", t=TILES)
    ids_v = ids.rearrange("(p t) f -> p t f", t=TILES)
    out_v = out.rearrange("(p t) o -> p (t o)", t=TILES)

    with ExitStack() as ctx:
        def sb(name, shape, dt=F32):
            return ctx.enter_context(nc.sbuf_tensor(name, shape, dt))

        def ps(name, shape):
            return ctx.enter_context(nc.psum_tensor(name, shape, F32))

        def sem(name):
            return ctx.enter_context(nc.semaphore(name))

        ident = sb("ident", [P, P])
        index = sb("index", [P, TILES, F], I32)
        rows = sb("rows", [P, HALVES, SLOTS, D])
        feat = sb("feat", [P, HALVES, P, QUADRANT])
        dense_t = sb("dense_t", [P, HALVES, P])
        gram = sb("gram", [P, SLOTS - 1, QUADS])
        pairs = sb("pairs", [QUADS, GROUPS, PAIR_ROWS])
        pairs_t = sb("pairs_t", [P, CHUNKS, P])
        h1 = sb("h1", [P, M1, P])
        h2 = sb("h2", [P, M2, P])
        w1_pairs = sb("w1_pairs", [P, CHUNKS, H1])
        w1_dense = sb("w1_dense", [P, 2, H1])
        w2 = sb("w2", [P, M1, H2])
        vectors = sb("vectors", [M1 + 2 * M2, P])
        columns = sb("columns", [P, M1 + 2 * M2])
        scores = sb("scores", [P, TILES])

        turned = ps("turned", [P, 2, PER_BANK, P])
        gram_ps = ps("gram_ps", [P, 2, PER_GRAM_BANK, QUADRANT])
        quads_ps = ps("quads_ps", [P, 2, PER_BANK, P])
        late = ps("late", [P, 512])
        h1_ps = ps("h1_ps", [P, M1, P])
        pairs_ps = late[:, 0:CHUNKS * P].rearrange("p (c b) -> p c b", c=CHUNKS)
        h2_ps = late[:, 0:M2 * P].rearrange("p (m b) -> p m b", m=M2)
        score_ps = late[:, 0:1]

        index_loaded = sem("index_loaded")
        dense_loaded = [sem(f"dense_loaded{h}") for h in range(HALVES)]
        lot_gathered = [[sem(f"lot_gathered{h}_{k}") for k in range(LOTS)] for h in range(HALVES)]
        w1_pairs_loaded = sem("w1_pairs_loaded")
        w1_dense_loaded = sem("w1_dense_loaded")
        w2_loaded = sem("w2_loaded")
        vectors_loaded = sem("vectors_loaded")
        ident_zeroed = sem("ident_zeroed")
        ident_ready = sem("ident_ready")
        w1_zeroed = sem("w1_zeroed")
        gram_zeroed = sem("gram_zeroed")
        columns_turned = sem("columns_turned")
        columns_ready = sem("columns_ready")
        lot_turned = sem("lot_turned")
        lot_even_kept = sem("lot_even_kept")
        lot_odd_kept = sem("lot_odd_kept")
        gram_made = sem("gram_made")
        gram_kept0 = sem("gram_kept0")
        gram_kept1 = sem("gram_kept1")
        quads_turned = sem("quads_turned")
        quads_even_kept = sem("quads_even_kept")
        quads_odd_kept = sem("quads_odd_kept")
        pairs_turned = sem("pairs_turned")
        pairs_kept = sem("pairs_kept")
        h1_made = sem("h1_made")
        h1_kept = sem("h1_kept")
        h2_made = sem("h2_made")
        h2_kept = sem("h2_kept")
        score_made = sem("score_made")
        score_kept = sem("score_kept")
        stored = sem("stored")

        block = ctx.enter_context(nc.Block())

        EVEN, ODD = (LOTS + 1) // 2, LOTS // 2
        bank_blocks = [[b for b in BLOCKS if b[0] // PER_BANK == k] for k in range(-(-(SLOTS - 1) // PER_BANK))]
        BANKS = len(bank_blocks)
        EVEN_B, ODD_B = (BANKS + 1) // 2, BANKS // 2

        def keep_lot(copy, half, k):
            s = lot(k)
            return copy(feat[:, half, :, s[0]:s[-1] + 1].rearrange("d b s -> d s b"),
                        turned[:, k % 2, 0:len(s), :])

        def keep_gram(copy, k):
            q = slice(PER_GRAM_BANK * k, PER_GRAM_BANK * (k + 1))
            return copy(gram[:, :, q].rearrange("p c q -> p q c"), gram_ps[:, k, :, 0:SLOTS - 1])

        def keep_quads(copy, k):
            for first, count, row, n, place in bank_blocks[k]:
                src = quads_ps[0:QUADS, k % 2, first % PER_BANK:first % PER_BANK + count, :]
                src = src.rearrange("q c (j s) -> q c j s", j=GROUPS)[:, :, :, row:row + n]
                dst = pairs[:, :, place:place + count * n].rearrange("q j (c s) -> q c j s", c=count)
                last = copy(dst, src)
            return last

        @block.sync
        def _(sp):
            sp.dma_start(index[:], ids_v).then_inc(index_loaded, 16)
            for half in range(HALVES):
                sp.dma_start(rows[:, half, 0, :], dense_v[:, half, :]).then_inc(dense_loaded[half], 16)
            vec = [(b_top1, M1), (b_top2, M2), (w_top3, M2)]
            at = 0
            for v, m in vec:
                src = v.rearrange("(m p) o -> m (p o)", m=m) if len(v.shape) == 2 else v.rearrange("(m p) -> m p", m=m)
                sp.dma_start(vectors[at:at + m, :], src).then_inc(vectors_loaded, 16)
                at += m
            sp.wait_ge(w1_zeroed, 1)
            for src, dst, n in weight_runs:
                sp.dma_start(w1_pairs[dst % P:dst % P + n, dst // P, :],
                             w_top1[src:src + n, :]).then_inc(w1_pairs_loaded, 16)
            for tile in range(HALVES, TILES):
                sp.wait_ge(lot_turned, LOTS * (tile - HALVES) + 1)
                sp.dma_start(rows[:, tile % HALVES, 0, :],
                             dense_v[:, tile, :]).then_inc(dense_loaded[tile % HALVES], 16)
            sp.wait_ge(score_kept, TILES)
            sp.dma_start(out_v, scores[:]).then_inc(stored, 16)
            sp.wait_ge(stored, 16)

        @block.gpsimd
        def _(pool):
            pool.wait_ge(ident_zeroed, 1)
            nc.gpsimd.affine_select(out=ident[:], in_=ident[:], compare_op=ALU.not_equal, fill=1.0, base=0,
                                    pattern=[[-1, P]], channel_multiplier=1).then_inc(ident_ready, 1)
            pool.wait_ge(index_loaded, 16)
            for tile in range(TILES):
                for f in range(F):
                    k = (f + 1) // PER_BANK
                    if tile >= HALVES and (f == 0 or (f + 1) % PER_BANK == 0):
                        pool.wait_ge(lot_turned, LOTS * (tile - HALVES) + k + 1)
                    nc.gpsimd.indirect_dma_start(
                        out=rows[:, tile % HALVES, f + 1, :], out_offset=None, in_=tables[f],
                        in_offset=bass.IndirectOffsetOnAxis(ap=index[:, tile, f:f + 1].bitcast(U32), axis=0),
                    ).then_inc(lot_gathered[tile % HALVES][k], 16)

        @block.tensor
        def _(pe):
            pe.wait_ge(ident_ready, 1)
            pe.wait_ge(vectors_loaded, 48)
            n = M1 + 2 * M2
            pe.transpose(late[:, 0:n], vectors[:], ident[0:n, 0:n]).then_inc(columns_turned, 1)
            for tile in range(TILES):
                half, turn = tile % HALVES, tile // HALVES
                for k in range(LOTS):
                    if k == 0:
                        pe.wait_ge(dense_loaded[half], 16 * (turn + 1))
                    gathers = len([s for s in lot(k) if s > 0])
                    pe.wait_ge(lot_gathered[half][k], 16 * gathers * (turn + 1))
                    if k >= 2:
                        pe.wait_ge([lot_even_kept, lot_odd_kept][k % 2], [EVEN, ODD][k % 2] * tile + k // 2)
                    else:
                        pe.wait_ge([lot_even_kept, lot_odd_kept][k % 2], [EVEN, ODD][k % 2] * tile)
                    for s in lot(k):
                        mm = pe.transpose(turned[:, k % 2, s % PER_BANK, :], rows[:, half, s, :], ident[:])
                    mm.then_inc(lot_turned, 1)
                pe.wait_ge(lot_even_kept, EVEN * (tile + 1))
                pe.wait_ge(lot_odd_kept, ODD * (tile + 1))
                if tile == 0:
                    pe.wait_ge(gram_zeroed, 1)
                for bank, kept in enumerate([gram_kept0, gram_kept1]):
                    pe.wait_ge(kept, tile)
                    for q in range(PER_GRAM_BANK):
                        for j in range(GROUPS):
                            f = feat[:, half, QUADS * j + PER_GRAM_BANK * bank + q, 0:SLOTS]
                            mm = pe.matmul(gram_ps[QUADRANT * j:QUADRANT * j + SLOTS, bank, q, 0:SLOTS], f, f,
                                           start=True, stop=True)
                    mm.then_inc(gram_made, 1)
                pe.wait_ge(gram_kept0, tile + 1)
                pe.wait_ge(gram_kept1, tile + 1)
                for k in range(BANKS):
                    kept, per = [(quads_even_kept, EVEN_B), (quads_odd_kept, ODD_B)][k % 2]
                    pe.wait_ge(kept, per * tile + k // 2)
                    for c in range(PER_BANK * k, min(PER_BANK * (k + 1), SLOTS - 1)):
                        mm = pe.transpose(quads_ps[0:QUADS, k % 2, c % PER_BANK, :], gram[:, c, :], ident[:])
                    mm.then_inc(quads_turned, 1)
                pe.wait_ge(quads_even_kept, EVEN_B * (tile + 1))
                pe.wait_ge(quads_odd_kept, ODD_B * (tile + 1))
                if tile == 0:
                    pe.wait_ge(columns_ready, 1)
                pe.wait_ge(score_kept, tile)
                for c in range(CHUNKS):
                    for j in range(GROUPS):
                        mm = pe.transpose(pairs_ps[:, c, QUADS * j:QUADS * (j + 1)],
                                          pairs[:, j, P * c:P * (c + 1)], ident[0:QUADS, 0:QUADS])
                mm.then_inc(pairs_turned, 1)
                if tile == 0:
                    pe.wait_ge(w1_dense_loaded, 32)
                    pe.wait_ge(w1_pairs_loaded, 16 * len(weight_runs))
                    pe.wait_ge(w2_loaded, 16)
                pe.wait_ge(pairs_kept, tile + 1)
                for m in range(M1):
                    for c in range(2):
                        pe.matmul(h1_ps[:, m, :], w1_dense[:, c, P * m:P * (m + 1)], dense_t[:, half, :],
                                  start=(c == 0), stop=False)
                    for c in range(CHUNKS):
                        mm = pe.matmul(h1_ps[:, m, :], w1_pairs[:, c, P * m:P * (m + 1)], pairs_t[:, c, :],
                                       start=False, stop=(c == CHUNKS - 1))
                mm.then_inc(h1_made, 1)
                pe.wait_ge(h1_kept, tile + 1)
                for m in range(M2):
                    for c in range(M1):
                        mm = pe.matmul(h2_ps[:, m, :], w2[:, c, P * m:P * (m + 1)], h1[:, c, :],
                                       start=(c == 0), stop=(c == M1 - 1))
                mm.then_inc(h2_made, 1)
                pe.wait_ge(h2_kept, tile + 1)
                for c in range(M2):
                    mm = pe.matmul(score_ps, h2[:, c, :], columns[:, M1 + M2 + c:M1 + M2 + c + 1],
                                   start=(c == 0), stop=(c == M2 - 1))
                mm.then_inc(score_made, 1)

        @block.vector
        def _(dve):
            nc.vector.memset(ident[:], 0.0).then_inc(ident_zeroed, 1)
            nc.vector.memset(w1_pairs[:], 0.0).then_inc(w1_zeroed, 1)
            nc.vector.memset(gram_ps[:], 0.0).then_inc(gram_zeroed, 1)
            dve.wait_ge(columns_turned, 1)
            nc.vector.tensor_copy(columns[:], late[:, 0:M1 + 2 * M2]).then_inc(columns_ready, 1)
            for tile in range(TILES):
                half = tile % HALVES
                for k in range(0, LOTS, 2):
                    dve.wait_ge(lot_turned, LOTS * tile + k + 1)
                    if tile >= HALVES and k == 0:
                        dve.wait_ge(gram_made, 2 * (tile - HALVES + 1))
                        dve.wait_ge(h1_made, tile - HALVES + 1)
                    if k == 0:
                        nc.vector.tensor_copy(dense_t[:, half, :], turned[:, 0, 0, :])
                    keep_lot(nc.vector.tensor_copy, half, k).then_inc(lot_even_kept, 1)
                dve.wait_ge(gram_made, 2 * tile + 1)
                if tile:
                    dve.wait_ge(quads_turned, BANKS * tile)
                keep_gram(nc.vector.tensor_copy, 0).then_inc(gram_kept0, 1)
                for k in range(0, BANKS, 2):
                    dve.wait_ge(quads_turned, BANKS * tile + k + 1)
                    if tile and k == 0:
                        dve.wait_ge(pairs_turned, tile)
                    keep_quads(nc.vector.tensor_copy, k).then_inc(quads_even_kept, 1)
                dve.wait_ge(pairs_turned, tile + 1)
                if tile:
                    dve.wait_ge(h1_made, tile)
                nc.vector.tensor_copy(pairs_t[:], pairs_ps).then_inc(pairs_kept, 1)
                dve.wait_ge(h2_made, tile + 1)
                if tile:
                    dve.wait_ge(score_made, tile)
                for m in range(M2):
                    last = nc.vector.tensor_scalar(h2[:, m, :], h2_ps[:, m, :], columns[:, M1 + m:M1 + m + 1], 0.0,
                                                   ALU.add, ALU.max)
                last.then_inc(h2_kept, 1)
                dve.wait_ge(score_made, tile + 1)
                nc.vector.tensor_copy(scores[:, tile:tile + 1], score_ps).then_inc(score_kept, 1)

        @block.scalar
        def _(act):
            for c, first in enumerate([0, DENSE1]):
                act.dma_start(w1_dense[:, c, :], w_top1[first:first + D, :]).then_inc(w1_dense_loaded, 16)
            act.dma_start(w2[:], w_top2.rearrange("(c p) n -> p c n", p=P)).then_inc(w2_loaded, 16)
            for tile in range(TILES):
                half = tile % HALVES
                for k in range(1, LOTS, 2):
                    act.wait_ge(lot_turned, LOTS * tile + k + 1)
                    if tile >= HALVES and k == 1:
                        act.wait_ge(gram_made, 2 * (tile - HALVES + 1))
                    keep_lot(nc.scalar.copy, half, k).then_inc(lot_odd_kept, 1)
                act.wait_ge(gram_made, 2 * tile + 2)
                if tile:
                    act.wait_ge(quads_turned, BANKS * tile)
                keep_gram(nc.scalar.copy, 1).then_inc(gram_kept1, 1)
                for k in range(1, BANKS, 2):
                    act.wait_ge(quads_turned, BANKS * tile + k + 1)
                    if tile and k == 1:
                        act.wait_ge(pairs_turned, tile)
                    keep_quads(nc.scalar.copy, k).then_inc(quads_odd_kept, 1)
                act.wait_ge(h1_made, tile + 1)
                if tile == 0:
                    act.wait_ge(columns_ready, 1)
                if tile:
                    act.wait_ge(h2_made, tile)
                for m in range(M1):
                    last = nc.scalar.activation(h1[:, m, :], h1_ps[:, m, :], ACT.Relu, bias=columns[:, m:m + 1])
                last.then_inc(h1_kept, 1)


def kernel(**inputs):
    import concourse.bacc as bacc
    from concourse.bass_utils import run_bass_kernel_spmd

    nc = bacc.Bacc("TRN2", target_bir_lowering=False, num_devices=1)
    arrays, aps = {}, {}
    for name, value in inputs.items():
        a = np.ascontiguousarray(value)
        arrays[f"in_{name}"] = a
        aps[name] = nc.dram_tensor(f"in_{name}", a.shape, mybir.dt.from_np(a.dtype), kind="ExternalInput").ap()
    batch, fields = inputs["ids"].shape
    out = nc.dram_tensor("scores_out", (batch, 1), F32, kind="ExternalOutput").ap()
    build_dlrm_tower(nc, aps["r_dense_features"], aps["ids"], [aps[f"tbl_{f}"] for f in range(fields)],
                     aps["W_top1"], aps["b_top1"], aps["W_top2"], aps["b_top2"], aps["W_top3"], out)
    r = run_bass_kernel_spmd(nc, [arrays], core_ids=[0])
    return r.results[0]["scores_out"]
```

```python
from contextlib import ExitStack

import numpy as np

import concourse.bass as bass
from concourse import mybir

F32 = mybir.dt.float32
BF16 = mybir.dt.bfloat16
F16 = mybir.dt.float16
I32 = mybir.dt.int32
U32 = mybir.dt.uint32
ALU = mybir.AluOpType
ACT = mybir.ActivationFunctionType

P = 128
PER_BANK = 4
QUADRANT = 32
GROUPS = P // QUADRANT


def column_groups(slots):
    out, place = [], 0
    for first, count in [(0, 2), (2, 2)] + [(c, 4) for c in range(4, slots - 3, 4)] + [(slots - 3, 2)]:
        rows = slots - 1 - first
        out.append((first, count, first + 1, rows, place))
        place += count * rows
    return out, place


def build_dlrm_tower(nc, dense, ids, tables, w_top1, b_top1, w_top2, b_top2, w_top3, out):
    B, D = dense.shape
    F = ids.shape[1]
    H1, H2 = w_top2.shape
    TILES = B // P
    PICKED = 5
    SLOTS = F + 1
    ROWS = SLOTS - PICKED
    LOTS = -(-ROWS // PER_BANK)
    QUADS = P // GROUPS
    PER_GRAM_BANK = QUADS // 2
    BLOCKS, PAIR_ROWS = column_groups(SLOTS)
    CHUNKS = PAIR_ROWS // P
    M1, M2 = H1 // P, H2 // P
    PAIRS0 = D
    DENSE1 = PAIRS0 + SLOTS * (SLOTS - 1) // 2
    VECTORS = M1 + 2 * M2
    picked = tables[F - PICKED:]
    CELLS = 8
    TABLE_P = picked[0].shape[0] // CELLS
    TABLE_BUFS = 3
    assert D == P and B == TILES * P and PAIR_ROWS == 3 * P and M1 == 4 and M2 == 2 and B == 512
    assert w_top1.shape[0] == DENSE1 + D
    assert all(t.shape[0] == TABLE_P * CELLS <= 2048 for t in picked) and TABLE_P <= P

    def lot(k):
        return range(PER_BANK * k, min(PER_BANK * (k + 1), ROWS))

    weight_runs = []
    for first, count, _, rows_, place in BLOCKS:
        for i in range(count):
            c = first + i
            src = PAIRS0 + sum(SLOTS - 1 - k for k in range(c))
            dst, n = place + i * rows_ + i, rows_ - i
            while n:
                m = min(n, P - dst % P)
                weight_runs.append((src, dst, m))
                src, dst, n = src + m, dst + m, n - m

    bank_blocks = [[b for b in BLOCKS if b[0] // PER_BANK == k] for k in range(-(-(SLOTS - 1) // PER_BANK))]
    BANKS = len(bank_blocks)
    chunk_banks = [1 + max(k for k in range(BANKS) for b in bank_blocks[k] if b[4] < P * (c + 1))
                   for c in range(CHUNKS)]

    EARLY = [LOTS * (x + 1) // PICKED - LOTS * x // PICKED for x in range(PICKED)]
    early = [[k for k in range(sum(EARLY[:x]), sum(EARLY[:x + 1]))] for x in range(PICKED)]

    dense_v = dense.rearrange("(p t) d -> p t d", t=TILES)
    ids_v = ids.rearrange("(p t) f -> p t f", t=TILES)
    out_v = out.rearrange("(p t) o -> p (t o)", t=TILES)

    with ExitStack() as ctx:
        def sb(name, shape, dt=F32):
            return ctx.enter_context(nc.sbuf_tensor(name, shape, dt))

        def ps(name, shape):
            return ctx.enter_context(nc.psum_tensor(name, shape, F32))

        def sem(name):
            return ctx.enter_context(nc.semaphore(name))

        ident = sb("ident", [P, P])
        index = sb("index", [P, TILES, F], I32)
        rows = sb("rows", [P, TILES, ROWS, D])
        feat = sb("feat", [P, TILES, P, SLOTS + 1])
        dense_t = sb("dense_t", [P, TILES, P])
        picked_ids = sb("picked_ids", [P, TILES, PICKED])
        id_rows = sb("id_rows", [PICKED, B], F16)
        spread = sb("spread", [PICKED, PICKED, TABLE_P], F16)
        row_number = sb("row_number", [TABLE_P, CELLS])
        id_wide = sb("id_wide", [TABLE_P, 2, B], F16)
        one_hot = sb("one_hot", [TABLE_P, 2, CELLS, B], BF16)
        table = sb("table", [TABLE_P, TABLE_BUFS, CELLS * D])
        beyond = sb("beyond", [TABLE_P, CELLS * D])
        high = sb("high", [TABLE_P, 2, CELLS * D], BF16)
        mid = sb("mid", [TABLE_P, 2, CELLS * D], BF16)
        low = sb("low", [TABLE_P, 2, CELLS * D], BF16)
        gram = sb("gram", [P, SLOTS - 1, QUADS])
        pairs = sb("pairs", [QUADS, GROUPS, PAIR_ROWS])
        pairs_t = sb("pairs_t", [P, CHUNKS, P])
        h1 = sb("h1", [P, M1, P])
        h2 = sb("h2", [P, M2, P])
        w1_pairs = sb("w1_pairs", [P, CHUNKS, H1])
        w1_dense2 = sb("w1_dense2", [P, 2, H1])
        w1_dense = sb("w1_dense", [P, H1])
        w2 = sb("w2", [P, M1, H2])
        vectors = sb("vectors", [VECTORS, P])
        columns = sb("columns", [P, VECTORS])
        scores = sb("scores", [P, TILES])

        turned = [ps(f"turned{i}", [P, PER_BANK, P]) for i in range(2)]
        product = [ps(f"product{i}", [P, PER_GRAM_BANK, QUADRANT]) for i in range(2)]
        quad = [ps(f"quad{i}", [P, PER_BANK, P]) for i in range(2)]
        late = ps("late", [P, 512])
        first = ps("first", [P, 512])
        id_wide_ps = [late, first]
        looked_up = [quad[i][:].rearrange("p a b -> p (a b)") for i in range(2)]
        pairs_ps = [product[0][:, 0:4, :].rearrange("p a b -> p (a b)"),
                    product[1][:, 0:4, :].rearrange("p a b -> p (a b)"), late[:, 0:P]]
        h1_ps = [first[:, 0:P], first[:, P:2 * P], turned[1][:, 0, :], turned[1][:, 1, :]]
        h2_ps = [late[:, 0:P], product[1][:, 0:4, :].rearrange("p a b -> p (a b)")]
        score_ps = late[:, 0:1]

        index_loaded = sem("index_loaded")
        dense_loaded = sem("dense_loaded")
        table_loaded = [sem(f"table_loaded{x}") for x in range(PICKED)]
        lot_gathered = [[sem(f"lot_gathered{t}_{k}") for k in range(LOTS)] for t in range(TILES)]
        w1_pairs_loaded = sem("w1_pairs_loaded")
        w1_dense_loaded = sem("w1_dense_loaded")
        w2_loaded = sem("w2_loaded")
        vectors_loaded = sem("vectors_loaded")
        ident_zeroed = sem("ident_zeroed")
        ident_ready = sem("ident_ready")
        row_number_ready = sem("row_number_ready")
        picked_ids_ready = sem("picked_ids_ready")
        id_rows_made = sem("id_rows_made")
        id_rows_kept = sem("id_rows_kept")
        spread_ready = sem("spread_ready")
        id_wide_made = sem("id_wide_made")
        id_wide_kept = sem("id_wide_kept")
        one_hot_made = sem("one_hot_made")
        high_made = sem("high_made")
        beyond_made = sem("beyond_made")
        mid_made = sem("mid_made")
        low_made = sem("low_made")
        looked_up_made = sem("looked_up_made")
        looked_up_kept = sem("looked_up_kept")
        w1_zeroed = sem("w1_zeroed")
        w1_summed = sem("w1_summed")
        product_zeroed = sem("product_zeroed")
        columns_turned = sem("columns_turned")
        columns_ready = sem("columns_ready")
        lot_turned = sem("lot_turned")
        lot_even_kept = sem("lot_even_kept")
        lot_odd_kept = sem("lot_odd_kept")
        product_made = sem("product_made")
        product0_kept = sem("product0_kept")
        product1_kept = sem("product1_kept")
        quads_turned = sem("quads_turned")
        quads_even_kept = sem("quads_even_kept")
        quads_odd_kept = sem("quads_odd_kept")
        pairs_turned = sem("pairs_turned")
        pairs_even_kept = sem("pairs_even_kept")
        pairs_odd_kept = sem("pairs_odd_kept")
        h1_low_made = sem("h1_low_made")
        h1_top_made = sem("h1_top_made")
        h1_low_kept = sem("h1_low_kept")
        h1_top_kept = sem("h1_top_kept")
        h2_made = sem("h2_made")
        h2_low_kept = sem("h2_low_kept")
        h2_top_kept = sem("h2_top_kept")
        score_made = sem("score_made")
        score_kept = sem("score_kept")
        stored = sem("stored")

        block = ctx.enter_context(nc.Block())

        EVEN, ODD = (LOTS + 1) // 2, LOTS // 2
        EVEN_B, ODD_B = (BANKS + 1) // 2, BANKS // 2
        EVEN_C, ODD_C = (CHUNKS + 1) // 2, CHUNKS // 2

        def keep_lot(copy, tile, k):
            s = lot(k)
            return copy(feat[:, tile, :, s[0]:s[-1] + 1].rearrange("d b s -> d s b"),
                        turned[k % 2][:, 0:len(s), :])

        def keep_product(copy, k):
            q = slice(PER_GRAM_BANK * k, PER_GRAM_BANK * (k + 1))
            return copy(gram[:, :, q].rearrange("p c q -> p q c"), product[k][:, :, 0:SLOTS - 1])

        def keep_quads(copy, k):
            for c0, count, row, n, place in bank_blocks[k]:
                src = quad[k % 2][0:QUADS, c0 % PER_BANK:c0 % PER_BANK + count, :]
                src = src.rearrange("q c (j s) -> q c j s", j=GROUPS)[:, :, :, row:row + n]
                dst = pairs[:, :, place:place + count * n].rearrange("q j (c s) -> q c j s", c=count)
                last = copy(dst, src)
            return last

        def load_table(eng, x):
            eng.dma_start(table[:, x % TABLE_BUFS, :],
                          picked[x].rearrange("(p c) d -> p (c d)", c=CELLS)).then_inc(table_loaded[x], 16)

        @block.sync
        def _(sp):
            sp.dma_start(index[:], ids_v).then_inc(index_loaded, 16)
            load_table(sp, 0)
            load_table(sp, 2)
            sp.dma_start(rows[:, :, 0, :], dense_v).then_inc(dense_loaded, 16)
            at = 0
            for v, m in [(b_top1, M1), (b_top2, M2), (w_top3, M2)]:
                flat = v.rearrange("n o -> (n o)") if len(v.shape) == 2 else v
                sp.dma_start(vectors[at:at + m, :],
                             flat.rearrange("(m p) -> m p", m=m)).then_inc(vectors_loaded, 16)
                at += m
            for x in range(TABLE_BUFS, PICKED):
                sp.wait_ge(beyond_made, x - TABLE_BUFS + 1)
                load_table(sp, x)
            for c, row in enumerate([0, DENSE1]):
                sp.dma_start(w1_dense2[:, c, :], w_top1[row:row + D, :]).then_inc(w1_dense_loaded, 16)
            sp.dma_start(w2[:], w_top2.rearrange("(c p) n -> p c n", p=P)).then_inc(w2_loaded, 16)
            sp.wait_ge(w1_zeroed, 1)
            for src, dst, n in weight_runs:
                sp.dma_start(w1_pairs[dst % P:dst % P + n, dst // P, :],
                             w_top1[src:src + n, :]).then_inc(w1_pairs_loaded, 16)
            sp.wait_ge(score_kept, TILES)
            sp.dma_start(out_v, scores[:]).then_inc(stored, 16)
            sp.wait_ge(stored, 16)

        @block.gpsimd
        def _(pool):
            pool.wait_ge(ident_zeroed, 1)
            nc.gpsimd.affine_select(out=ident[:], in_=ident[:], compare_op=ALU.not_equal, fill=1.0, base=0,
                                    pattern=[[-1, P]], channel_multiplier=1).then_inc(ident_ready, 1)
            nc.gpsimd.iota(row_number[:], pattern=[[1, CELLS]], base=0, channel_multiplier=CELLS,
                           allow_small_or_imprecise_dtypes=True).then_inc(row_number_ready, 1)
            pool.wait_ge(index_loaded, 16)
            for tile in range(TILES):
                for s in range(1, ROWS):
                    nc.gpsimd.indirect_dma_start(
                        out=rows[:, tile, s, :], out_offset=None, in_=tables[s - 1],
                        in_offset=bass.IndirectOffsetOnAxis(ap=index[:, tile, s - 1:s].bitcast(U32), axis=0),
                    ).then_inc(lot_gathered[tile][s // PER_BANK], 16)

        @block.tensor
        def _(pe):
            pe.wait_ge(ident_ready, 1)
            pe.wait_ge(picked_ids_ready, 1)
            for tile in range(TILES):
                mm = pe.transpose(late[0:PICKED, P * tile:P * (tile + 1)], picked_ids[:, tile, :], ident[:])
            mm.then_inc(id_rows_made, 1)

            def widen(x):
                if x >= 2:
                    pe.wait_ge(id_wide_kept, x - 1)
                pe.matmul(id_wide_ps[x % 2][0:TABLE_P, :], spread[:, x, :], id_rows[:],
                          start=True, stop=True).then_inc(id_wide_made, 1)

            def look_up(x):
                if x >= 2:
                    pe.wait_ge(looked_up_kept, x - 1)
                pe.wait_ge(one_hot_made, x + 1)
                for n, (part, made) in enumerate([(high, high_made), (mid, mid_made), (low, low_made)]):
                    pe.wait_ge(made, x + 1)
                    for c in range(CELLS):
                        mm = pe.matmul(looked_up[x % 2], part[:, x % 2, D * c:D * (c + 1)],
                                       one_hot[:, x % 2, c, :], start=(n == 0 and c == 0),
                                       stop=(n == 2 and c == CELLS - 1))
                mm.then_inc(looked_up_made, 1)

            def turn_lot(tile, k):
                if tile == 0 and k == 0:
                    pe.wait_ge(dense_loaded, 16)
                pe.wait_ge(lot_gathered[tile][k], 16 * len([s for s in lot(k) if s > 0]))
                if k % 2:
                    pe.wait_ge(lot_odd_kept, ODD * tile + k // 2)
                else:
                    pe.wait_ge(lot_even_kept, EVEN * tile + k // 2)
                for s in lot(k):
                    mm = pe.transpose(turned[k % 2][:, s % PER_BANK, :], rows[:, tile, s, :], ident[:])
                mm.then_inc(lot_turned, 1)

            def multiply(tile):
                pe.wait_ge(lot_even_kept, EVEN * (tile + 1))
                pe.wait_ge(lot_odd_kept, ODD * (tile + 1))
                if tile == 0:
                    pe.wait_ge(looked_up_kept, PICKED)
                    pe.wait_ge(product_zeroed, 1)
                for bank in range(2):
                    for q in range(PER_GRAM_BANK):
                        for j in range(GROUPS):
                            f = feat[:, tile, QUADS * j + PER_GRAM_BANK * bank + q, 0:SLOTS]
                            mm = pe.matmul(product[bank][QUADRANT * j:QUADRANT * j + SLOTS, q, 0:SLOTS], f, f,
                                           start=True, stop=True)
                    mm.then_inc(product_made, 1)

            def turn_products(tile):
                pe.wait_ge(product0_kept, tile + 1)
                pe.wait_ge(product1_kept, tile + 1)
                if tile == 0:
                    pe.wait_ge(columns_ready, 1)
                chunk = 0
                for k in range(BANKS + 2):
                    if k < BANKS:
                        if k % 2:
                            pe.wait_ge(quads_odd_kept, ODD_B * tile + k // 2)
                        else:
                            pe.wait_ge(quads_even_kept, EVEN_B * tile + k // 2)
                        for c in range(PER_BANK * k, min(PER_BANK * (k + 1), SLOTS - 1)):
                            mm = pe.transpose(quad[k % 2][0:QUADS, c % PER_BANK, :], gram[:, c, :], ident[:])
                        mm.then_inc(quads_turned, 1)
                    while chunk < CHUNKS and chunk_banks[chunk] <= k - 1:
                        n = chunk_banks[chunk]
                        pe.wait_ge(quads_even_kept, EVEN_B * tile + (n + 1) // 2)
                        pe.wait_ge(quads_odd_kept, ODD_B * tile + n // 2)
                        for j in range(GROUPS):
                            mm = pe.transpose(pairs_ps[chunk][:, QUADS * j:QUADS * (j + 1)],
                                              pairs[:, j, P * chunk:P * (chunk + 1)], ident[0:QUADS, 0:QUADS])
                        mm.then_inc(pairs_turned, 1)
                        chunk += 1

            def layer1_dense(tile):
                if tile == 0:
                    pe.wait_ge(w1_summed, 1)
                pe.wait_ge(lot_odd_kept, ODD * (tile + 1) + (tile + 1 < TILES))
                for m in range(M1):
                    pe.matmul(h1_ps[m], w1_dense[:, P * m:P * (m + 1)], dense_t[:, tile, :],
                              start=(m % 2 == 0), stop=False, skip_group_check=True)

            def layer1_pairs(tile):
                if tile == 0:
                    pe.wait_ge(w1_pairs_loaded, 16 * len(weight_runs))
                for c in range(CHUNKS):
                    if c % 2:
                        pe.wait_ge(pairs_odd_kept, ODD_C * tile + c // 2 + 1)
                    else:
                        pe.wait_ge(pairs_even_kept, EVEN_C * tile + c // 2 + 1)
                    for m in range(M1):
                        mm = pe.matmul(h1_ps[m], w1_pairs[:, c, P * m:P * (m + 1)], pairs_t[:, c, :],
                                       start=False, stop=(c == CHUNKS - 1), skip_group_check=True)
                        if c == CHUNKS - 1 and m == 1:
                            mm.then_inc(h1_low_made, 1)
                mm.then_inc(h1_top_made, 1)

            def layer2(tile):
                if tile == 0:
                    pe.wait_ge(w2_loaded, 16)
                for c in range(M1):
                    if c == 0:
                        pe.wait_ge(h1_low_kept, tile + 1)
                    if c == 2:
                        pe.wait_ge(h1_top_kept, tile + 1)
                    for m in range(M2):
                        mm = pe.matmul(h2_ps[m], w2[:, c, P * m:P * (m + 1)], h1[:, c, :],
                                       start=(c == 0), stop=(c == M1 - 1))
                mm.then_inc(h2_made, 1)

            def layer3(tile):
                pe.wait_ge(h2_low_kept, tile + 1)
                pe.wait_ge(h2_top_kept, tile + 1)
                if tile:
                    pe.wait_ge(score_kept, tile)
                for c in range(M2):
                    mm = pe.matmul(score_ps, h2[:, c, :], columns[:, M1 + M2 + c:M1 + M2 + c + 1],
                                   start=(c == 0), stop=(c == M2 - 1))
                mm.then_inc(score_made, 1)

            pe.wait_ge(spread_ready, 1)
            pe.wait_ge(id_rows_kept, 1)
            widen(0)
            for x in range(PICKED):
                if x + 1 < PICKED:
                    widen(x + 1)
                look_up(x)
                for k in early[x]:
                    turn_lot(0, k)
            pe.wait_ge(id_wide_kept, PICKED)
            pe.wait_ge(vectors_loaded, 48)
            pe.transpose(late[:, 0:VECTORS], vectors[:], ident[0:VECTORS, 0:VECTORS]).then_inc(columns_turned, 1)
            for tile in range(TILES - 1):
                multiply(tile)
                turn_lot(tile + 1, 0)
                turn_lot(tile + 1, 1)
                turn_products(tile)
                turn_lot(tile + 1, 2)
                layer1_dense(tile)
                layer1_pairs(tile)
                layer2(tile)
                turn_lot(tile + 1, 3)
                layer3(tile)
                for k in range(4, LOTS):
                    turn_lot(tile + 1, k)
            multiply(TILES - 1)
            layer1_dense(TILES - 1)
            turn_products(TILES - 1)
            layer1_pairs(TILES - 1)
            layer2(TILES - 1)
            layer3(TILES - 1)

        @block.vector
        def _(dve):
            nc.vector.memset(ident[:], 0.0).then_inc(ident_zeroed, 1)
            dve.wait_ge(ident_ready, 1)
            nc.vector.tensor_copy(spread[:], ident[0:PICKED, 0:PICKED].unsqueeze(2)
                                  .to_broadcast([PICKED, PICKED, TABLE_P])).then_inc(spread_ready, 1)
            dve.wait_ge(index_loaded, 16)
            nc.vector.tensor_copy(picked_ids[:], index[:, :, F - PICKED:F]).then_inc(picked_ids_ready, 1)
            dve.wait_ge(id_rows_made, 1)
            nc.vector.tensor_copy(id_rows[:], late[0:PICKED, :]).then_inc(id_rows_kept, 1)
            dve.wait_ge(row_number_ready, 1)
            def keep_even_lot(tile, k):
                dve.wait_ge(lot_turned, LOTS * tile + k + 1)
                if k == 0:
                    nc.vector.tensor_copy(dense_t[:, tile, :], turned[0][:, 0, :])
                keep_lot(nc.vector.tensor_copy, tile, k).then_inc(lot_even_kept, 1)

            for x in range(PICKED):
                dve.wait_ge(id_wide_kept, x + 1)
                if x >= 2:
                    dve.wait_ge(looked_up_made, x - 1)
                for c in range(CELLS):
                    last = nc.vector.tensor_scalar(one_hot[:, x % 2, c, :], id_wide[:, x % 2, :],
                                                   row_number[:, c:c + 1], None, ALU.is_equal)
                last.then_inc(one_hot_made, 1)
                dve.wait_ge(high_made, x + 1)
                if x:
                    dve.wait_ge(low_made, x)
                nc.vector.tensor_tensor(beyond[:], table[:, x % TABLE_BUFS, :], high[:, x % 2, :],
                                        ALU.subtract).then_inc(beyond_made, 1)
                dve.wait_ge(mid_made, x + 1)
                nc.vector.tensor_tensor(low[:, x % 2, :], beyond[:], mid[:, x % 2, :],
                                        ALU.subtract).then_inc(low_made, 1)
                if x == 0:
                    nc.vector.memset(w1_pairs[:], 0.0).then_inc(w1_zeroed, 1)
                    nc.vector.memset(product[0][:], 0.0)
                    nc.vector.memset(product[1][:], 0.0).then_inc(product_zeroed, 1)
                else:
                    for k in early[x - 1]:
                        if k % 2 == 0:
                            keep_even_lot(0, k)
            for k in early[PICKED - 1]:
                if k % 2 == 0:
                    keep_even_lot(0, k)
            dve.wait_ge(w1_dense_loaded, 32)
            nc.vector.tensor_tensor(w1_dense[:], w1_dense2[:, 0, :], w1_dense2[:, 1, :],
                                    ALU.add).then_inc(w1_summed, 1)
            dve.wait_ge(columns_turned, 1)
            nc.vector.tensor_copy(columns[:], late[:, 0:VECTORS]).then_inc(columns_ready, 1)
            for tile in range(TILES):
                following = tile + 1 < TILES
                dve.wait_ge(product_made, 2 * tile + 1)
                if tile:
                    dve.wait_ge(quads_turned, BANKS * tile)
                keep_product(nc.vector.tensor_copy, 0).then_inc(product0_kept, 1)
                if following:
                    keep_even_lot(tile + 1, 0)
                steps = [("q", k) for k in range(0, BANKS, 2)]
                for c in range(0, CHUNKS, 2):
                    at = [i for i, s in enumerate(steps) if s[0] == "q" and s[1] < chunk_banks[c]][-1] + 2
                    steps.insert(at, ("p", c))
                for kind, k in steps:
                    if kind == "q":
                        dve.wait_ge(quads_turned, BANKS * tile + k + 1)
                        if tile and k == 0:
                            dve.wait_ge(pairs_turned, CHUNKS * tile)
                        keep_quads(nc.vector.tensor_copy, k).then_inc(quads_even_kept, 1)
                    else:
                        dve.wait_ge(pairs_turned, CHUNKS * tile + k + 1)
                        if tile and k == 0:
                            dve.wait_ge(h1_top_made, tile)
                        nc.vector.tensor_copy(pairs_t[:, k, :], pairs_ps[k]).then_inc(pairs_even_kept, 1)
                if following:
                    keep_even_lot(tile + 1, 2)
                dve.wait_ge(h1_top_made, tile + 1)
                if tile:
                    dve.wait_ge(h2_made, tile)
                for m in range(2, M1):
                    last = nc.vector.tensor_scalar(h1[:, m, :], h1_ps[m], columns[:, m:m + 1], 0.0,
                                                   ALU.add, ALU.max)
                last.then_inc(h1_top_kept, 1)
                dve.wait_ge(h2_made, tile + 1)
                if tile:
                    dve.wait_ge(score_made, tile)
                nc.vector.tensor_scalar(h2[:, 1, :], h2_ps[1], columns[:, M1 + 1:M1 + 2], 0.0,
                                        ALU.add, ALU.max).then_inc(h2_top_kept, 1)
                dve.wait_ge(score_made, tile + 1)
                nc.vector.tensor_copy(scores[:, tile:tile + 1], score_ps).then_inc(score_kept, 1)
                if following:
                    for k in range(4, LOTS, 2):
                        keep_even_lot(tile + 1, k)

        @block.scalar
        def _(act):
            load_table(act, 1)

            def keep_looked_up(x):
                act.wait_ge(looked_up_made, x + 1)
                nc.scalar.copy(feat[:, :, :, ROWS + x].rearrange("d t b -> d (t b)"),
                               looked_up[x % 2]).then_inc(looked_up_kept, 1)

            def keep_odd_lot(tile, k):
                act.wait_ge(lot_turned, LOTS * tile + k + 1)
                keep_lot(nc.scalar.copy, tile, k).then_inc(lot_odd_kept, 1)

            for x in range(PICKED):
                act.wait_ge(id_wide_made, x + 1)
                if x >= 2:
                    act.wait_ge(one_hot_made, x - 1)
                nc.scalar.copy(id_wide[:, x % 2, :], id_wide_ps[x % 2][0:TABLE_P, :]).then_inc(id_wide_kept, 1)
                act.wait_ge(table_loaded[x], 16)
                if x >= 2:
                    act.wait_ge(looked_up_made, x - 1)
                nc.scalar.copy(high[:, x % 2, :], table[:, x % TABLE_BUFS, :]).then_inc(high_made, 1)
                act.wait_ge(beyond_made, x + 1)
                nc.scalar.copy(mid[:, x % 2, :], beyond[:]).then_inc(mid_made, 1)
                if x:
                    keep_looked_up(x - 1)
                    for k in early[x - 1]:
                        if k % 2:
                            keep_odd_lot(0, k)
            keep_looked_up(PICKED - 1)
            for k in early[PICKED - 1]:
                if k % 2:
                    keep_odd_lot(0, k)
            for tile in range(TILES):
                following = tile + 1 < TILES
                act.wait_ge(product_made, 2 * tile + 2)
                if tile:
                    act.wait_ge(quads_turned, BANKS * tile)
                keep_product(nc.scalar.copy, 1).then_inc(product1_kept, 1)
                if following:
                    keep_odd_lot(tile + 1, 1)
                for k in range(1, BANKS, 2):
                    act.wait_ge(quads_turned, BANKS * tile + k + 1)
                    if tile and k == 1:
                        act.wait_ge(pairs_turned, CHUNKS * tile)
                    keep_quads(nc.scalar.copy, k).then_inc(quads_odd_kept, 1)
                act.wait_ge(pairs_turned, CHUNKS * tile + 2)
                if tile:
                    act.wait_ge(h1_top_made, tile)
                nc.scalar.copy(pairs_t[:, 1, :], pairs_ps[1]).then_inc(pairs_odd_kept, 1)
                act.wait_ge(h1_low_made, tile + 1)
                if tile == 0:
                    act.wait_ge(columns_ready, 1)
                else:
                    act.wait_ge(h2_made, tile)
                for m in range(2):
                    last = nc.scalar.activation(h1[:, m, :], h1_ps[m], ACT.Relu, bias=columns[:, m:m + 1])
                last.then_inc(h1_low_kept, 1)
                act.wait_ge(h2_made, tile + 1)
                if tile:
                    act.wait_ge(score_made, tile)
                nc.scalar.activation(h2[:, 0, :], h2_ps[0], ACT.Relu,
                                     bias=columns[:, M1:M1 + 1]).then_inc(h2_low_kept, 1)
                if following:
                    for k in range(3, LOTS, 2):
                        keep_odd_lot(tile + 1, k)


def kernel(**inputs):
    import concourse.bacc as bacc
    from concourse.bass_utils import run_bass_kernel_spmd

    nc = bacc.Bacc("TRN2", target_bir_lowering=False, num_devices=1)
    arrays, aps = {}, {}
    for name, value in inputs.items():
        a = np.ascontiguousarray(value)
        arrays[f"in_{name}"] = a
        aps[name] = nc.dram_tensor(f"in_{name}", a.shape, mybir.dt.from_np(a.dtype), kind="ExternalInput").ap()
    batch, fields = inputs["ids"].shape
    out = nc.dram_tensor("scores_out", (batch, 1), F32, kind="ExternalOutput").ap()
    build_dlrm_tower(nc, aps["r_dense_features"], aps["ids"], [aps[f"tbl_{f}"] for f in range(fields)],
                     aps["W_top1"], aps["b_top1"], aps["W_top2"], aps["b_top2"], aps["W_top3"], out)
    r = run_bass_kernel_spmd(nc, [arrays], core_ids=[0])
    return r.results[0]["scores_out"]
```

```python
from contextlib import ExitStack

import numpy as np

import concourse.bass as bass
from concourse import mybir

F32 = mybir.dt.float32
F32R = mybir.dt.float32r
F16 = mybir.dt.float16
I32 = mybir.dt.int32
U32 = mybir.dt.uint32
ALU = mybir.AluOpType
ACT = mybir.ActivationFunctionType

P = 128
PER_BANK = 4
QUADRANT = 32
GROUPS = P // QUADRANT


def build_dlrm_tower(nc, dense, ids, tables, w_top1, b_top1, w_top2, b_top2, w_top3, out):
    B, D = dense.shape
    F = ids.shape[1]
    H1, H2 = w_top2.shape
    TILES = B // P
    PICKED = 8
    SLOTS = F + 1
    ROWS = SLOTS - PICKED
    LOTS = -(-ROWS // PER_BANK)
    QUADS = P // GROUPS
    PER_GRAM_BANK = QUADS // 2
    COLUMNS = SLOTS - 1
    PAIRS = SLOTS * (SLOTS - 1) // 2
    CHUNKS = -(-PAIRS // P)
    M1, M2 = H1 // P, H2 // P
    LAST = TILES - 1
    PAIRS0 = D
    DENSE1 = PAIRS0 + PAIRS
    VECTORS = M1 + 2 * M2
    picked = tables[F - PICKED:]
    CELLS = 8
    TABLE_P = picked[0].shape[0] // CELLS
    TABLE_BUFS = 3
    ACT_CELLS = [1 + x % 2 for x in range(PICKED)]
    DVE_CELLS = [CELLS - n for n in ACT_CELLS]
    assert D == P and B == TILES * P and CHUNKS == 3 and M1 == 4 and M2 == 2 and B == 512
    assert w_top1.shape[0] == DENSE1 + D
    assert all(t.shape[0] == TABLE_P * CELLS <= 2048 for t in picked) and TABLE_P <= P

    def lot(k):
        return range(PER_BANK * k, min(PER_BANK * (k + 1), ROWS))

    pair_place = [sum(COLUMNS - k for k in range(c)) for c in range(COLUMNS)]
    chunk_rows = [min(P, PAIRS - P * c) for c in range(CHUNKS)]

    BATCHES = -(-COLUMNS // GROUPS)
    batch_columns = [range(GROUPS * k, min(GROUPS * (k + 1), COLUMNS)) for k in range(BATCHES)]
    chunk_batches = [1 + max(k for k in range(BATCHES) if pair_place[batch_columns[k][0]] < P * (c + 1))
                     for c in range(CHUNKS)]

    early = [range(LOTS * x // (PICKED - 1), LOTS * (x + 1) // (PICKED - 1)) for x in range(PICKED - 1)]

    def following_lots(tile, stage):
        if tile == LAST:
            return []
        before = 1 if tile == LAST - 1 else LOTS
        counts = {"start": 2 if tile == 0 else 0, "products": 2, "pairs": 1, "before layer 2": before,
                  "after layer 2": LOTS}
        at = 0
        for name, n in counts.items():
            if name == stage:
                return list(range(at, min(at + n, LOTS)))
            at += n

    dense_v = dense.rearrange("(p t) d -> p t d", t=TILES)
    ids_v = ids.rearrange("(p t) f -> p t f", t=TILES)
    out_v = out.rearrange("(p t) o -> p (t o)", t=TILES)

    with ExitStack() as ctx:
        def sb(name, shape, dt=F32):
            return ctx.enter_context(nc.sbuf_tensor(name, shape, dt))

        def ps(name, shape):
            return ctx.enter_context(nc.psum_tensor(name, shape, F32))

        def sem(name):
            return ctx.enter_context(nc.semaphore(name))

        ident = sb("ident", [P, P])
        index = sb("index", [P, TILES, F], I32)
        rows = sb("rows", [P, TILES, ROWS, D])
        feat = sb("feat", [P, TILES, P, SLOTS + 1])
        dense_t = sb("dense_t", [P, TILES, P])
        picked_ids = sb("picked_ids", [P, TILES, PICKED], F16)
        ident_half = sb("ident_half", [P, P], F16)
        row_number = sb("row_number", [TABLE_P, CELLS])
        id_wide = sb("id_wide", [TABLE_P, 2, B], F16)
        distance = sb("distance", [TABLE_P, max(ACT_CELLS), B], F16)
        one_hot = sb("one_hot", [TABLE_P, 2, CELLS, B], F32R)
        table = sb("table", [TABLE_P, TABLE_BUFS, CELLS * D])
        high = sb("high", [TABLE_P, 2, CELLS * D], F32R)
        low = sb("low", [TABLE_P, 2, CELLS * D], F32R)
        gram = sb("gram", [P, COLUMNS, QUADS])
        pairs = sb("pairs", [QUADS, GROUPS, PAIRS])
        pairs_t = sb("pairs_t", [P, CHUNKS, P])
        h1 = sb("h1", [P, M1, P])
        h2 = sb("h2", [P, TILES, M2, P])
        w1_pairs = sb("w1_pairs", [P, CHUNKS, H1])
        w1_dense2 = sb("w1_dense2", [P, 2, H1])
        w1_dense = sb("w1_dense", [P, H1])
        w2 = sb("w2", [P, M1, H2])
        vectors = sb("vectors", [VECTORS, P])
        columns = sb("columns", [P, VECTORS])
        scores = sb("scores", [P, TILES])

        turned = [ps(f"turned{i}", [P, PER_BANK, P]) for i in range(2)]
        product = [ps(f"product{i}", [P, PER_GRAM_BANK, QUADRANT]) for i in range(2)]
        quad = [ps(f"quad{i}", [P, PER_BANK, GROUPS, QUADRANT]) for i in range(2)]
        sums2 = ps("sums2", [P, 512])
        sums1 = ps("sums1", [P, 512])
        id_wide_ps = [sums2, sums1]
        looked_up = [quad[i][:].rearrange("p a j s -> p (a j s)") for i in range(2)]
        pairs_ps = [product[0][:, 0:4, :].rearrange("p a b -> p (a b)"),
                    product[1][:, 0:4, :].rearrange("p a b -> p (a b)"), sums2[:, 0:P]]
        h1_ps = [[sums1[:, P * m:P * (m + 1)] for m in range(M1)]] * LAST + [
            [sums1[:, 0:P], sums1[:, P:2 * P], turned[1][:, 0, :], turned[1][:, 1, :]]]
        h1_starts = [(0,)] * LAST + [(0, 2)]
        h2_ps = [[sums2[:, P * m:P * (m + 1)] for m in range(M2)]] * LAST + [
            [sums2[:, 0:P], product[1][:, 0:4, :].rearrange("p a b -> p (a b)")]]
        h2_starts = [(0,)] * LAST + [(0, 1)]
        score_ps = turned[0][:, 0, 0:TILES]

        index_loaded = sem("index_loaded")
        dense_loaded = sem("dense_loaded")
        table_loaded = [sem(f"table_loaded{x}") for x in range(PICKED)]
        lot_gathered = [[sem(f"lot_gathered{t}_{k}") for k in range(LOTS)] for t in range(TILES)]
        w1_pairs_loaded = sem("w1_pairs_loaded")
        w1_dense_loaded = sem("w1_dense_loaded")
        w2_loaded = sem("w2_loaded")
        vectors_loaded = sem("vectors_loaded")
        ident_zeroed = sem("ident_zeroed")
        ident_ready = sem("ident_ready")
        row_number_ready = sem("row_number_ready")
        picked_ids_ready = sem("picked_ids_ready")
        ident_half_ready = sem("ident_half_ready")
        id_wide_made = sem("id_wide_made")
        id_wide_kept = sem("id_wide_kept")
        one_hot_made = sem("one_hot_made")
        distance_made = sem("distance_made")
        one_hot_top_made = sem("one_hot_top_made")
        high_made = sem("high_made")
        low_made = sem("low_made")
        looked_up_made = sem("looked_up_made")
        looked_up_kept = sem("looked_up_kept")
        w1_summed = sem("w1_summed")
        product_zeroed = sem("product_zeroed")
        columns_turned = sem("columns_turned")
        columns_ready = sem("columns_ready")
        lot_turned = sem("lot_turned")
        lot_even_kept = sem("lot_even_kept")
        lot_odd_kept = sem("lot_odd_kept")
        product_made = sem("product_made")
        product0_kept = sem("product0_kept")
        product1_kept = sem("product1_kept")
        quads_turned = sem("quads_turned")
        quads_even_kept = sem("quads_even_kept")
        quads_odd_kept = sem("quads_odd_kept")
        pairs_turned = sem("pairs_turned")
        pairs_even_kept = sem("pairs_even_kept")
        pairs_odd_kept = sem("pairs_odd_kept")
        h1_made = sem("h1_made")
        h1_kept = sem("h1_kept")
        h1_top_kept = sem("h1_top_kept")
        h2_made = sem("h2_made")
        h2_kept = sem("h2_kept")
        h2_top_kept = sem("h2_top_kept")
        score_made = sem("score_made")
        score_kept = sem("score_kept")
        stored = sem("stored")

        block = ctx.enter_context(nc.Block())

        EVEN, ODD = (LOTS + 1) // 2, LOTS // 2
        EVEN_B, ODD_B = (BATCHES + 1) // 2, BATCHES // 2
        EVEN_C, ODD_C = (CHUNKS + 1) // 2, CHUNKS // 2

        def keep_lot(copy, tile, k):
            s = lot(k)
            return copy(feat[:, tile, :, s[0]:s[-1] + 1].rearrange("d b s -> d s b"),
                        turned[k % 2][:, 0:len(s), :])

        def keep_product(copy, k):
            q = slice(PER_GRAM_BANK * k, PER_GRAM_BANK * (k + 1))
            return copy(gram[:, :, q].rearrange("p c q -> p q c"), product[k][:, :, 0:COLUMNS])

        def keep_batch(copy, k):
            for i, c in enumerate(batch_columns[k]):
                last = copy(pairs[:, :, pair_place[c]:pair_place[c] + COLUMNS - c],
                            quad[k % 2][QUADS * i:QUADS * (i + 1), k // 2, :, c + 1:SLOTS])
            return last

        def load_table(eng, x):
            eng.dma_start(table[:, x % TABLE_BUFS, :],
                          picked[x].rearrange("(p c) d -> p (c d)", c=CELLS)).then_inc(table_loaded[x], 16)

        @block.sync
        def _(sp):
            sp.dma_start(index[:], ids_v).then_inc(index_loaded, 16)
            load_table(sp, 1)
            load_table(sp, 2)
            sp.dma_start(rows[:, :, 0, :], dense_v).then_inc(dense_loaded, 16)
            at = 0
            for v, m in [(b_top1, M1), (b_top2, M2), (w_top3, M2)]:
                flat = v.rearrange("n o -> (n o)") if len(v.shape) == 2 else v
                sp.dma_start(vectors[at:at + m, :],
                             flat.rearrange("(m p) -> m p", m=m)).then_inc(vectors_loaded, 16)
                at += m
            for x in range(TABLE_BUFS, PICKED):
                sp.wait_ge(low_made, x - TABLE_BUFS + 1)
                load_table(sp, x)
            for c, row in enumerate([0, DENSE1]):
                sp.dma_start(w1_dense2[:, c, :], w_top1[row:row + D, :]).then_inc(w1_dense_loaded, 16)
            sp.dma_start(w2[:], w_top2.rearrange("(c p) n -> p c n", p=P)).then_inc(w2_loaded, 16)
            for c, n in enumerate(chunk_rows):
                row = PAIRS0 + P * c
                sp.dma_start(w1_pairs[0:n, c, :], w_top1[row:row + n, :]).then_inc(w1_pairs_loaded, 16)
            sp.wait_ge(score_kept, 1)
            sp.dma_start(out_v, scores[:]).then_inc(stored, 16)
            sp.wait_ge(stored, 16)

        @block.gpsimd
        def _(pool):
            pool.wait_ge(ident_zeroed, 1)
            nc.gpsimd.affine_select(out=ident[:], in_=ident[:], compare_op=ALU.not_equal, fill=1.0, base=0,
                                    pattern=[[-1, P]], channel_multiplier=1).then_inc(ident_ready, 1)
            nc.gpsimd.iota(row_number[:], pattern=[[1, CELLS]], base=0, channel_multiplier=CELLS,
                           allow_small_or_imprecise_dtypes=True).then_inc(row_number_ready, 1)
            pool.wait_ge(index_loaded, 16)
            for tile in range(TILES):
                for s in range(1, ROWS):
                    nc.gpsimd.indirect_dma_start(
                        out=rows[:, tile, s, :], out_offset=None, in_=tables[s - 1],
                        in_offset=bass.IndirectOffsetOnAxis(ap=index[:, tile, s - 1:s].bitcast(U32), axis=0),
                    ).then_inc(lot_gathered[tile][s // PER_BANK], 16)

        @block.tensor
        def _(pe):
            def widen(x):
                if x >= 2:
                    pe.wait_ge(id_wide_kept, x - 1)
                for tile in range(TILES):
                    mm = pe.matmul(id_wide_ps[x % 2][0:TABLE_P, P * tile:P * (tile + 1)],
                                   picked_ids[:, tile, x:x + 1].to_broadcast([P, TABLE_P]), ident_half[:],
                                   start=True, stop=True)
                mm.then_inc(id_wide_made, 1)

            def look_up(x):
                if x >= 2:
                    pe.wait_ge(looked_up_kept, x - 1)
                for n, (part, made) in enumerate([(high, high_made), (low, low_made)]):
                    pe.wait_ge(made, x + 1)
                    for c in range(CELLS):
                        if n == 0:
                            if c < DVE_CELLS[x]:
                                pe.wait_ge(one_hot_made, sum(DVE_CELLS[:x]) + c + 1)
                            else:
                                pe.wait_ge(one_hot_top_made, x + 1)
                        mm = pe.matmul(looked_up[x % 2], part[:, x % 2, D * c:D * (c + 1)],
                                       one_hot[:, x % 2, c, :], start=(n == 0 and c == 0),
                                       stop=(n == 1 and c == CELLS - 1))
                mm.then_inc(looked_up_made, 1)

            def turn_lot(tile, k):
                if tile == 0 and k == 0:
                    pe.wait_ge(dense_loaded, 16)
                pe.wait_ge(lot_gathered[tile][k], 16 * len([s for s in lot(k) if s > 0]))
                if k % 2:
                    pe.wait_ge(lot_odd_kept, ODD * tile + k // 2)
                else:
                    pe.wait_ge(lot_even_kept, EVEN * tile + k // 2)
                for s in lot(k):
                    mm = pe.transpose(turned[k % 2][:, s % PER_BANK, :], rows[:, tile, s, :], ident[:])
                mm.then_inc(lot_turned, 1)

            def multiply(tile, bank):
                if bank == 0:
                    pe.wait_ge(lot_even_kept, EVEN * (tile + 1))
                    pe.wait_ge(lot_odd_kept, ODD * (tile + 1))
                if tile == 0:
                    pe.wait_ge(looked_up_kept, PICKED)
                    pe.wait_ge(product_zeroed, 1)
                for q in range(PER_GRAM_BANK):
                    for j in range(GROUPS):
                        f = feat[:, tile, QUADS * j + PER_GRAM_BANK * bank + q, 0:SLOTS]
                        mm = pe.matmul(product[bank][QUADRANT * j:QUADRANT * j + SLOTS, q, 0:SLOTS], f, f,
                                       start=True, stop=True)
                mm.then_inc(product_made, 1)

            def turn_batches(tile, parity):
                if parity:
                    pe.wait_ge(quads_odd_kept, ODD_B * tile)
                else:
                    pe.wait_ge(product0_kept, tile + 1)
                    pe.wait_ge(product1_kept, tile + 1)
                    pe.wait_ge(quads_even_kept, EVEN_B * tile)
                for k in range(parity, BATCHES, 2):
                    cols = batch_columns[k]
                    mm = pe.transpose(quad[parity][0:QUADS * len(cols), k // 2, :, :]
                                      .rearrange("p j s -> p (j s)"),
                                      gram[:, cols[0]:cols[-1] + 1, :].rearrange("p c q -> p (c q)"), ident[:])
                mm.then_inc(quads_turned, 1)

            def turn_pairs(tile, c):
                n, height = chunk_batches[c], chunk_rows[c]
                pe.wait_ge(quads_even_kept, EVEN_B * tile + (n + 1) // 2)
                pe.wait_ge(quads_odd_kept, ODD_B * tile + n // 2)
                if c == 2:
                    if tile:
                        pe.wait_ge(h2_kept, tile)
                    else:
                        pe.wait_ge(columns_ready, 1)
                for j in range(GROUPS):
                    mm = pe.transpose(pairs_ps[c][0:height, QUADS * j:QUADS * (j + 1)],
                                      pairs[:, j, P * c:P * c + height], ident[0:QUADS, 0:QUADS])
                mm.then_inc(pairs_turned, 1)

            def layer1_dense(tile, blocks):
                if blocks[0] == 0 and tile == 0:
                    pe.wait_ge(w1_summed, 1)
                elif blocks[0] == 0:
                    pe.wait_ge(h1_kept, M1 * tile)
                for m in blocks:
                    pe.matmul(h1_ps[tile][m], w1_dense[:, P * m:P * (m + 1)], dense_t[:, tile, :],
                              start=(m in h1_starts[tile]), stop=False, skip_group_check=True)

            def layer1_pairs(tile, c):
                if tile == 0 and c == 0:
                    pe.wait_ge(w1_pairs_loaded, 16 * CHUNKS)
                if c % 2:
                    pe.wait_ge(pairs_odd_kept, ODD_C * tile + c // 2 + 1)
                else:
                    pe.wait_ge(pairs_even_kept, EVEN_C * tile + c // 2 + 1)
                height = chunk_rows[c]
                for m in range(M1):
                    mm = pe.matmul(h1_ps[tile][m], w1_pairs[0:height, c, P * m:P * (m + 1)], pairs_t[0:height, c, :],
                                   start=False, stop=(c == CHUNKS - 1), skip_group_check=True)
                    if c == CHUNKS - 1 and (m == M1 - 1 or m + 1 in h1_starts[tile]):
                        mm.then_inc(h1_made, 1)

            def layer2(tile):
                if tile == 0:
                    pe.wait_ge(w2_loaded, 16)
                for c in range(M1):
                    if tile == LAST and c >= 2:
                        pe.wait_ge(h1_top_kept, c - 1)
                    else:
                        pe.wait_ge(h1_kept, M1 * tile + c + 1)
                    for m in range(M2):
                        mm = pe.matmul(h2_ps[tile][m], w2[:, c, P * m:P * (m + 1)], h1[:, c, :],
                                       start=(c == 0 and m in h2_starts[tile]), stop=(c == M1 - 1),
                                       skip_group_check=True)
                mm.then_inc(h2_made, 1)

            def layer3(tile):
                pe.wait_ge(h2_kept, tile + 1)
                if tile == LAST:
                    pe.wait_ge(h2_top_kept, 1)
                for c in range(M2):
                    mm = pe.matmul(score_ps[:, tile:tile + 1], h2[:, tile, c, :],
                                   columns[:, M1 + M2 + c:M1 + M2 + c + 1], start=(c == 0), stop=(c == M2 - 1))
                mm.then_inc(score_made, 1)

            pe.wait_ge(ident_half_ready, 1)
            pe.wait_ge(picked_ids_ready, 1)
            widen(0)
            for x in range(PICKED):
                if x + 1 < PICKED:
                    widen(x + 1)
                look_up(x)
                if x < PICKED - 1:
                    for k in early[x]:
                        turn_lot(0, k)
            pe.wait_ge(id_wide_kept, PICKED)
            pe.wait_ge(vectors_loaded, 48)
            pe.transpose(sums2[:, 0:VECTORS], vectors[:], ident[0:VECTORS, 0:VECTORS]).then_inc(columns_turned, 1)
            for tile in range(LAST):
                for k in following_lots(tile, "start"):
                    turn_lot(tile + 1, k)
                multiply(tile, 0)
                multiply(tile, 1)
                for k in following_lots(tile, "products"):
                    turn_lot(tile + 1, k)
                layer1_dense(tile, range(0, 2))
                turn_batches(tile, 0)
                turn_batches(tile, 1)
                layer1_dense(tile, range(2, M1))
                for k in following_lots(tile, "pairs"):
                    turn_lot(tile + 1, k)
                turn_pairs(tile, 0)
                turn_pairs(tile, 1)
                layer1_pairs(tile, 0)
                turn_pairs(tile, 2)
                layer1_pairs(tile, 1)
                layer1_pairs(tile, 2)
                for k in following_lots(tile, "before layer 2"):
                    turn_lot(tile + 1, k)
                layer2(tile)
                for k in following_lots(tile, "after layer 2"):
                    turn_lot(tile + 1, k)
            layer1_dense(LAST, range(0, 2))
            multiply(LAST, 0)
            multiply(LAST, 1)
            layer1_dense(LAST, range(2, M1))
            turn_batches(LAST, 0)
            turn_batches(LAST, 1)
            for tile in range(LAST - 1):
                layer3(tile)
            turn_pairs(LAST, 0)
            turn_pairs(LAST, 1)
            layer1_pairs(LAST, 0)
            turn_pairs(LAST, 2)
            layer1_pairs(LAST, 1)
            layer1_pairs(LAST, 2)
            layer2(LAST)
            layer3(LAST - 1)
            layer3(LAST)

        @block.vector
        def _(dve):
            nc.vector.memset(ident[:], 0.0).then_inc(ident_zeroed, 1)
            dve.wait_ge(ident_ready, 1)
            nc.vector.tensor_copy(ident_half[:], ident[:]).then_inc(ident_half_ready, 1)
            dve.wait_ge(index_loaded, 16)
            nc.vector.tensor_copy(picked_ids[:], index[:, :, F - PICKED:F]).then_inc(picked_ids_ready, 1)
            dve.wait_ge(row_number_ready, 1)

            def keep_even_lot(tile, k):
                dve.wait_ge(lot_turned, LOTS * tile + k + 1)
                if k == 0:
                    nc.vector.tensor_copy(dense_t[:, tile, :], turned[0][:, 0, :])
                keep_lot(nc.vector.tensor_copy, tile, k).then_inc(lot_even_kept, 1)

            for x in range(PICKED):
                dve.wait_ge(id_wide_kept, x + 1)
                if x >= 2:
                    dve.wait_ge(looked_up_made, x - 1)
                for c in range(DVE_CELLS[x]):
                    nc.vector.tensor_scalar(one_hot[:, x % 2, c, :], id_wide[:, x % 2, :], row_number[:, c:c + 1],
                                            None, ALU.is_equal).then_inc(one_hot_made, 1)
                dve.wait_ge(high_made, x + 1)
                nc.vector.tensor_tensor(low[:, x % 2, :], table[:, x % TABLE_BUFS, :], high[:, x % 2, :],
                                        ALU.subtract).then_inc(low_made, 1)
                if x:
                    for k in early[x - 1]:
                        if k % 2 == 0:
                            keep_even_lot(0, k)
            nc.vector.memset(product[0][:], 0.0)
            nc.vector.memset(product[1][:], 0.0).then_inc(product_zeroed, 1)
            dve.wait_ge(w1_dense_loaded, 32)
            nc.vector.tensor_tensor(w1_dense[:], w1_dense2[:, 0, :], w1_dense2[:, 1, :],
                                    ALU.add).then_inc(w1_summed, 1)
            dve.wait_ge(columns_turned, 1)
            nc.vector.tensor_copy(columns[:], sums2[:, 0:VECTORS]).then_inc(columns_ready, 1)

            def keep_even_batch(tile, k):
                dve.wait_ge(quads_turned, 2 * tile + 1)
                if tile and k == 0:
                    dve.wait_ge(pairs_turned, CHUNKS * tile)
                keep_batch(nc.vector.tensor_copy, k).then_inc(quads_even_kept, 1)

            def keep_even_pairs(tile, c):
                dve.wait_ge(pairs_turned, CHUNKS * tile + c + 1)
                if tile and c == 0:
                    dve.wait_ge(h1_made, tile)
                nc.vector.tensor_copy(pairs_t[0:chunk_rows[c], c, :],
                                      pairs_ps[c][0:chunk_rows[c], :]).then_inc(pairs_even_kept, 1)

            def keep_even_lots(tile, stage):
                for k in following_lots(tile, stage):
                    if k % 2 == 0:
                        keep_even_lot(tile + 1, k)

            for tile in range(TILES):
                keep_even_lots(tile, "start")
                dve.wait_ge(product_made, 2 * tile + 1)
                if tile:
                    dve.wait_ge(quads_turned, 2 * tile)
                keep_product(nc.vector.tensor_copy, 0).then_inc(product0_kept, 1)
                keep_even_lots(tile, "products")
                keep_even_batch(tile, 0)
                keep_even_batch(tile, 2)
                keep_even_pairs(tile, 0)
                keep_even_batch(tile, 4)
                keep_even_batch(tile, 6)
                keep_even_lots(tile, "pairs")
                keep_even_pairs(tile, 2)
                keep_even_lots(tile, "before layer 2")
                keep_even_lots(tile, "after layer 2")
            dve.wait_ge(h1_made, LAST + 2)
            dve.wait_ge(h2_made, LAST)
            for m in range(2, M1):
                nc.vector.tensor_scalar(h1[:, m, :], h1_ps[LAST][m], columns[:, m:m + 1], 0.0,
                                        ALU.add, ALU.max).then_inc(h1_top_kept, 1)
            dve.wait_ge(h2_made, LAST + 1)
            nc.vector.tensor_scalar(h2[:, LAST, 1, :], h2_ps[LAST][1], columns[:, M1 + 1:M1 + 2], 0.0,
                                    ALU.add, ALU.max).then_inc(h2_top_kept, 1)
            dve.wait_ge(score_made, TILES)
            nc.vector.tensor_copy(scores[:], score_ps).then_inc(score_kept, 1)

        @block.scalar
        def _(act):
            load_table(act, 0)

            def keep_looked_up(x):
                act.wait_ge(looked_up_made, x + 1)
                nc.scalar.copy(feat[:, :, :, ROWS + x].rearrange("d t b -> d (t b)"),
                               looked_up[x % 2]).then_inc(looked_up_kept, 1)

            def keep_odd_lot(tile, k):
                act.wait_ge(lot_turned, LOTS * tile + k + 1)
                keep_lot(nc.scalar.copy, tile, k).then_inc(lot_odd_kept, 1)

            for x in range(PICKED):
                act.wait_ge(id_wide_made, x + 1)
                if x >= 2:
                    act.wait_ge(one_hot_made, sum(DVE_CELLS[:x - 1]))
                    act.wait_ge(one_hot_top_made, x - 1)
                nc.scalar.copy(id_wide[:, x % 2, :], id_wide_ps[x % 2][0:TABLE_P, :]).then_inc(id_wide_kept, 1)
                act.wait_ge(table_loaded[x], 16)
                if x >= 2:
                    act.wait_ge(looked_up_made, x - 1)
                nc.scalar.copy(high[:, x % 2, :], table[:, x % TABLE_BUFS, :]).then_inc(high_made, 1)
                act.wait_ge(id_wide_kept, x + 1)
                if x == 0:
                    act.wait_ge(row_number_ready, 1)
                else:
                    act.wait_ge(one_hot_top_made, x)
                for c in range(ACT_CELLS[x]):
                    nc.scalar.activation(distance[:, c, :], id_wide[:, x % 2, :], ACT.Abs, scale=-1.0,
                                         bias=row_number[:, DVE_CELLS[x] + c:DVE_CELLS[x] + c + 1]
                                         ).then_inc(distance_made, 1)
                act.wait_ge(distance_made, sum(ACT_CELLS[:x + 1]))
                nc.scalar.activation(one_hot[:, x % 2, DVE_CELLS[x]:CELLS, :].rearrange("p c b -> p (c b)"),
                                     distance[:, 0:ACT_CELLS[x], :].rearrange("p c b -> p (c b)"), ACT.Relu, scale=-1.0,
                                     bias=1.0).then_inc(one_hot_top_made, 1)
                if x:
                    keep_looked_up(x - 1)
                    for k in early[x - 1]:
                        if k % 2:
                            keep_odd_lot(0, k)
            keep_looked_up(PICKED - 1)

            def keep_odd_lots(tile, stage):
                for k in following_lots(tile, stage):
                    if k % 2:
                        keep_odd_lot(tile + 1, k)

            for tile in range(TILES):
                keep_odd_lots(tile, "start")
                act.wait_ge(product_made, 2 * tile + 2)
                if tile:
                    act.wait_ge(quads_turned, 2 * tile)
                keep_product(nc.scalar.copy, 1).then_inc(product1_kept, 1)
                keep_odd_lots(tile, "products")
                act.wait_ge(quads_turned, 2 * tile + 2)
                if tile:
                    act.wait_ge(pairs_turned, CHUNKS * tile)
                for k in range(1, BATCHES, 2):
                    keep_batch(nc.scalar.copy, k).then_inc(quads_odd_kept, 1)
                keep_odd_lots(tile, "pairs")
                act.wait_ge(pairs_turned, CHUNKS * tile + 2)
                if tile:
                    act.wait_ge(h1_made, tile)
                nc.scalar.copy(pairs_t[:, 1, :], pairs_ps[1]).then_inc(pairs_odd_kept, 1)
                act.wait_ge(h1_made, tile + 1)
                if tile == 0:
                    act.wait_ge(columns_ready, 1)
                else:
                    act.wait_ge(h2_made, tile)
                for m in range(M1 if tile < LAST else 2):
                    nc.scalar.activation(h1[:, m, :], h1_ps[tile][m], ACT.Relu,
                                         bias=columns[:, m:m + 1]).then_inc(h1_kept, 1)
                keep_odd_lots(tile, "before layer 2")
                act.wait_ge(h2_made, tile + 1)
                for m in range(M2 if tile < LAST else 1):
                    last = nc.scalar.activation(h2[:, tile, m, :], h2_ps[tile][m], ACT.Relu,
                                                bias=columns[:, M1 + m:M1 + m + 1])
                last.then_inc(h2_kept, 1)
                keep_odd_lots(tile, "after layer 2")


def kernel(**inputs):
    import concourse.bacc as bacc
    from concourse.bass_utils import run_bass_kernel_spmd

    nc = bacc.Bacc("TRN2", target_bir_lowering=False, num_devices=1)
    arrays, aps = {}, {}
    for name, value in inputs.items():
        a = np.ascontiguousarray(value)
        arrays[f"in_{name}"] = a
        aps[name] = nc.dram_tensor(f"in_{name}", a.shape, mybir.dt.from_np(a.dtype), kind="ExternalInput").ap()
    batch, fields = inputs["ids"].shape
    out = nc.dram_tensor("scores_out", (batch, 1), F32, kind="ExternalOutput").ap()
    build_dlrm_tower(nc, aps["r_dense_features"], aps["ids"], [aps[f"tbl_{f}"] for f in range(fields)],
                     aps["W_top1"], aps["b_top1"], aps["W_top2"], aps["b_top2"], aps["W_top3"], out)
    r = run_bass_kernel_spmd(nc, [arrays], core_ids=[0])
    return r.results[0]["scores_out"]
```
